# Optimizing a Trainium2 kernel written in Bass

```python
import numpy as np
import jax
import jax.numpy as jnp

def _softmax(x, axis=-1):
    return jax.nn.softmax(x, axis=axis)
def _gelu(x):
    return jax.nn.gelu(x, approximate=True)
def _silu(x):
    return jax.nn.silu(x)
def _sigmoid(x):
    return jax.nn.sigmoid(x)
def _layernorm(x, axis=-1, eps=1e-5):
    m = jnp.mean(x, axis=axis, keepdims=True)
    v = jnp.var(x, axis=axis, keepdims=True)
    return (x - m) / jnp.sqrt(v + eps)
def _scatter_add(tgt, idx, src, axis=0):
    return tgt.at[idx].add(src)
def _segment_sum(src, seg, n):
    return jax.ops.segment_sum(src, seg, n)

kernel_name = 'mk_adj_preln_d1_adj_256_281715'

def setup_inputs(seed: int = 0):
    np.random.seed(seed)
    _w = jnp.asarray
    def _rec_inputs():
        import jax
        import jax.numpy as jnp
        _gk = jax.random.key(seed)
        x = -0.0005207 + 1.001 * jax.random.normal(jax.random.fold_in(_gk, 1), (8192, 256), jnp.float32)
        _a = jax.random.bernoulli(jax.random.fold_in(_gk, 2), 0.00195312, (8192, 8192))
        _a = jnp.logical_or(_a, jnp.eye(8192, dtype=bool))
        _af = _a.astype(jnp.float32)
        adj = _af
        return x, adj
    x, adj = _rec_inputs()
    def _L0_gnn_setup():
        import jax, jax.numpy as jnp
        import numpy as np
        N = 8192
        F = 256
        NEG_INF = -9000000000000000.0
        ALPHA = 0.2
        THRESH = 1e-06
        key = jax.random.key(seed)
        k1, k2, k3, k4 = jax.random.split(key, 4)
        x = jax.random.normal(k1, (N, F), jnp.float32)
        h0 = jax.random.normal(k2, (N, F), jnp.float32)
        limit = float(np.sqrt(6.0 / (2 * F + 1)) * 1.414)
        a = jax.random.uniform(k3, (2 * F, 1), jnp.float32, -limit, limit)
        temp = jnp.zeros((5,), jnp.float32)
        adj = jax.random.bernoulli(k4, 0.005, (N, N)).astype(jnp.float32)
        adj = jnp.maximum(adj, jnp.eye(N, dtype=jnp.float32))
        return {'x': x, 'h0': h0, 'a': a, 'temp': temp, 'adj': adj, 'l': 1}
    _L0_gnn_all = _L0_gnn_setup()
    _L0_gnn_in = {k: v for k, v in _L0_gnn_all.items() if k in ('h0', 'a', 'temp', )}
    del _L0_gnn_all

    return {
        "x": x,
        "adj": adj,
        "L0_gnn_h0": _L0_gnn_in["h0"],
        "L0_gnn_a": _L0_gnn_in["a"],
        "L0_gnn_temp": _L0_gnn_in["temp"],
    }

def reference(x, adj, L0_gnn_h0, L0_gnn_a, L0_gnn_temp):
    import jax
    import jax.numpy as jnp
    def _L0_gnn_ref(x, h0, a, temp, adj, l):
        import jax, jax.numpy as jnp
        import numpy as np
        N = 8192
        F = 256
        NEG_INF = -9000000000000000.0
        ALPHA = 0.2
        THRESH = 1e-06
        Fdim = x.shape[1]
        feat_1 = x @ a[:Fdim]
        feat_2 = x @ a[Fdim:]
        e = jax.nn.leaky_relu(feat_1 + feat_2.T, ALPHA)
        att = jnp.where(adj > 0, e, NEG_INF)
        U = jax.nn.softmax(att, axis=1)
        P = 0.5 * U
        prop_u = U @ x
        rowsum = jnp.sum(U * P, axis=1)
        coe = jax.nn.sigmoid(temp)
        xi = x * rowsum[:, None]
        feat_odd = prop_u - xi
        feat_even = x + prop_u - xi
        feat = coe[2] * feat_odd + (1.0 - coe[2]) * feat_even
        sgn = jnp.sign(feat)
        mod = jnp.abs(feat)
        mod = jnp.where(mod > THRESH, mod - THRESH, 0.0)
        feat = mod * sgn
        pu = U @ feat
        feat_odd2 = feat - coe[3] * pu
        feat_even2 = pu + feat_odd2 * rowsum[:, None]
        feat_odd2 = coe[0] * feat_odd2 + (1.0 - coe[0]) * h0
        out = coe[1] * feat_even2 + (1.0 - coe[1]) * feat_odd2
        return out

    h = jnp.maximum(_layernorm(x, axis=-1), 0.0)
    x = x + _L0_gnn_ref(h, L0_gnn_h0, L0_gnn_a, L0_gnn_temp, adj, 1)
    return x


_drawn_inputs = setup_inputs


def setup_inputs(seed=0):
    import zlib

    import numpy as np

    out = dict(_drawn_inputs(seed))
    spreads = {'L0_gnn_temp': (0.0, 0.8)}
    factors = {}
    for name, (base, spread) in spreads.items():
        noise = np.random.default_rng([zlib.crc32(name.encode()), seed]).standard_normal(out[name].shape)
        drawn = base * np.exp(spread * noise) if base else spread * noise
        out[name] = jnp.asarray(drawn.astype(out[name].dtype))
    for name, factor in factors.items():
        out[name] = (out[name] * factor).astype(out[name].dtype)
    return out
```

```python
import concourse.bass as bass
from concourse import mybir
from contextlib import ExitStack


def graph_attention_layer(nc, x, adj, h0, a, temp, out):
    F32, F16, F8 = mybir.dt.float32, mybir.dt.float16, mybir.dt.float8e4
    ALU = mybir.AluOpType
    ACT = mybir.ActivationFunctionType
    AX = mybir.AxisListType

    P = 128
    N, F = x.shape
    TILES = N // P
    GROUP = 1024
    GPT = N // GROUP
    QPG = GROUP // P
    PAIRS = TILES // 2
    STEPS = 2 * GPT
    GROUPS = TILES * GPT
    CHUNK = 2 * GROUP
    CPT = N // CHUNK
    ADJ_SLOTS = 2
    PAIR_SLOTS = 4
    XG = 8
    NXG = TILES // XG
    BLK = 4
    NBLK = TILES // BLK

    ALPHA, EPS, THRESH = 0.2, 1e-5, 1e-6
    H_SCALE = 2.0 ** 11
    U_SCALE = 2.0 ** 15
    FEAT_SCALE = 2.0 ** 10

    HI_LAG = 3
    SPLIT_LAG = GPT + 4
    STORE_LAG = SPLIT_LAG + 4
    BY_SCALAR = (3, 7)
    E1_AT = 5
    E2_AT = 6
    MM_LAG = 3

    hs_dram = nc.dram_tensor("hs_scratch", (TILES, P, F), F32, kind="Internal").ap()
    ut_dram = nc.dram_tensor("ut_scratch", (TILES * GPT, P, 2 * GROUP), F16, kind="Internal").ap()
    fh_dram = nc.dram_tensor("feat_pair_scratch", (TILES, P, 2 * F), F16, kind="Internal").ap()
    ft_dram = nc.dram_tensor("feat_scratch", (TILES, P, F + 1), F32, kind="Internal").ap()
    x_t = x.rearrange("(t p) f -> t p f", p=P)
    h0_t = h0.rearrange("(t p) f -> t p f", p=P)
    out_t = out.rearrange("(t p) f -> t p f", p=P)
    adj_t = adj.rearrange("(t p) (g c) -> t g p c", p=P, c=GROUP)

    ctx = ExitStack()
    with ctx:
        def sb(name, shape, dt=F32):
            return ctx.enter_context(nc.sbuf_tensor(name, shape, dt))

        def pb(name, shape):
            return ctx.enter_context(nc.psum_tensor(name, shape, F32))

        def sem(name):
            return ctx.enter_context(nc.semaphore(name))

        rows = sb("rows", [P, 2, N])
        row_b, row_q = rows[:, 0, :], rows[:, 1, :]
        vbuf = sb("vbuf", [P, 2, N])
        xpair = sb("xpair", [P, TILES, 2 * F], F16)
        adj_sb = sb("adj_sb", [P, ADJ_SLOTS, GROUP])
        pair = sb("pair", [P, PAIR_SLOTS, 2, GROUP], F16)
        junk = sb("junk", [P, CHUNK], F8)
        pu = sb("pu", [P, F])
        hrow = sb("hrow", [P, F + 1])
        fpair = sb("fpair", [P, 2 * F], F16)
        ident = sb("ident", [P, P])
        neg_ident = sb("neg_ident", [P, P], F16)
        c_all = sb("c_all", [P, TILES])
        vs = sb("vs", [P, 2, GPT])
        sq_part = sb("sq_part", [P, 2, CPT])
        small = sb("small", [P, 40])
        vsum, wden = small[:, 0:1], small[:, 1:2]
        rnorm = [small[:, 2 + i:3 + i] for i in range(2)]
        rbias = [small[:, 4 + i:5 + i] for i in range(2)]
        two_sq, s_row = small[:, 6:8], small[:, 8:9]
        gmax, ngmax, ngmax_q, gmax_c = (small[:, 9 + i:10 + i] for i in range(4))
        sig = small[:, 13:18]
        c1, nc3, m2s, k0, k_a, k_i = (small[:, 18 + i:19 + i] for i in range(6))
        om1, om0 = small[:, 24:25], small[:, 25:26]
        sq_sum = small[:, 26:27]
        acol = small[:, 28:32]

        acc = [pb(f"acc{i}", [P, 2 * F]) for i in range(2)]
        ps_t = [pb(f"ps_t{i}", [P, GROUP]) for i in range(2)]
        ps_f1 = pb("ps_f1", [P, TILES])

        xs = vbuf[:, :, :].rearrange("p a (t f) -> p (a t) f", f=F)
        stats = row_b[:, 0:TILES * 6].rearrange("p (t s) -> p t s", s=6)
        mv = row_b[:, TILES * 6:TILES * 8].rearrange("p (t s) -> p t s", s=2)
        ve, rstd, ytmp, hsc, nbias = (row_b[:, TILES * (8 + i):TILES * (9 + i)] for i in range(5))
        gblk = pu[:, 0:NBLK]
        h_t = [pair[:, i, :, :].rearrange("p a c -> p (a c)").bitcast(F32) for i in range(2)]
        a2_wide = hrow[:, 0:F].rearrange("p (k m) -> p k m", m=P)
        fx = rows[:, :, :].rearrange("p a n -> p (a n)").bitcast(F16).rearrange("p (t f) -> p t f", f=2 * F)
        ut_sb = vbuf[:, :, :].rearrange("p a n -> p (a n)").bitcast(F16).rearrange("p (s c) -> p s c", c=4 * GROUP)
        ep = pair[:, :, :, :].rearrange("p s a c -> p (s a c)").bitcast(F32)[:, 0:8 * (F + 4)].rearrange(
            "p (s k f) -> p s k f", s=2, f=F + 4)

        names = """res_done act_waited pool_waited scratch_out id_done acol_in temp_in stats_done aggr_done ve_done sd_done rstd_chain nb_done relu_done
            split_done ht_ps ht_sb f2_ps f1_done f2_sb blk_max gm_chain row_done c_done a2_done
            sig_e coef_chain t_done v_done den_chain r_done norm_done sq_done tr_done hi_done lo_v lo_s
            mm_done e1_done pu_done pool_chain feat_done hs_in mm2_done e3_done
            out_done out_chain""".split()
        S = {n: sem(n) for n in names}
        x_in = [sem(f"x_in{i}") for i in range(NXG)]
        adj_in = [sem(f"adj_in{i}") for i in range(ADJ_SLOTS)]
        ut_out = [sem(f"ut_out{i}") for i in range(PAIR_SLOTS)]
        UT_SLOTS = 8
        QPT = GPT // 2
        ut_in = [sem(f"ut_in{i}") for i in range(UT_SLOTS)]
        fx_in = [sem(f"fx_in{i}") for i in range(NXG)]
        ep_in = [sem(f"ep_in{i}") for i in range(2)]
        o_out = [sem(f"o_out{i}") for i in range(2)]

        HS_STORED = 16 * NXG
        def wait_lo(eng, u, m):
            t, g = 2 * u + m // GPT, m % GPT
            by_s = [i for i in range(g + 1) if i in BY_SCALAR]
            if g in BY_SCALAR:
                eng.wait_ge(S["lo_s"], len(BY_SCALAR) * t + len(by_s))
            else:
                eng.wait_ge(S["lo_v"], (GPT - len(BY_SCALAR)) * t + g + 1 - len(by_s))

        POOL_OPS = 10

        def pairs(eng, step, lag):
            for k in range(STEPS):
                step(0, k, True, True)
            with eng.Fori(1, PAIRS) as u:
                for k in range(STEPS):
                    step(u, k, False, True)
            for k in range(STEPS, STEPS + lag):
                step(PAIRS - 1, k, False, False)

        block = ctx.enter_context(nc.Block())

        @block.sync
        def _(sp):
            for g in range(NXG):
                sp.dma_start(xs[:, g * XG:(g + 1) * XG, :],
                             x_t[g * XG:(g + 1) * XG].rearrange("t p f -> p t f")).then_inc(x_in[g], 16)
            for g in range(ADJ_SLOTS):
                sp.dma_start(adj_sb[:, g, :], adj_t[0, g]).then_inc(adj_in[g], 16)
            for g in range(NXG):
                sp.wait_ge(S["relu_done"], XG * (g + 1))
                sp.dma_start(hs_dram[g * XG:(g + 1) * XG].rearrange("t p f -> p t f"),
                             xs[:, g * XG:(g + 1) * XG, :]).then_inc(S["scratch_out"], 16)
            sp.wait_ge(S["scratch_out"], 16 * NXG)

            def step(u, k, first, fill):
                if fill and not (first and k < ADJ_SLOTS):
                    sp.wait_ge(S["v_done"], STEPS * u + k - ADJ_SLOTS + 1)
                    sp.dma_start(adj_sb[:, k % ADJ_SLOTS, :], adj_t[2 * u + k // GPT, k % GPT])\
                        .then_inc(adj_in[k % ADJ_SLOTS], 16)
                m = k - STORE_LAG
                if (not first or m >= 0) and m < STEPS:
                    wait_lo(sp, u, m)
                    sp.dma_start(ut_dram[STEPS * u + m], pair[:, m % PAIR_SLOTS].rearrange("p a c -> p (a c)"))\
                        .then_inc(ut_out[m % PAIR_SLOTS], 16)
                s = k // GPT - 2
                if not first or s >= 0:
                    t = 2 * u + s
                    if k % GPT == 3:
                        sp.wait_ge(S["scratch_out"], HS_STORED + 32 * t)
                        sp.dma_start(hrow[:, 0:F], hs_dram[t]).then_inc(S["hs_in"], 16)

            pairs(sp, step, STEPS)

            def load_fx(g):
                if g == 0:
                    sp.wait_ge(S["t_done"], GROUPS // 2)
                sp.wait_ge(S["scratch_out"], HS_STORED + 32 * XG * (g + 1))
                sp.dma_start(fx[:, g * XG:(g + 1) * XG, :],
                             fh_dram[g * XG:(g + 1) * XG].rearrange("t p f -> p t f")).then_inc(fx_in[g], 16)

            def load_ut(v, q, first):
                if not first:
                    sp.wait_ge(S["mm2_done"], UT_SLOTS * v + q - UT_SLOTS + 1)
                sp.dma_start(ut_sb[:, q, :].rearrange("p (g c) -> p g c", g=2),
                             ut_dram[bass.ds(STEPS * v + 2 * q, 2)].rearrange("g p c -> p g c"))\
                    .then_inc(ut_in[q], 16)

            def load_ep(v, par, first):
                t = 2 * v + par
                if not first:
                    sp.wait_ge(S["out_done"], t - 1)
                for i, src in enumerate((x_t[t], h0_t[t])):
                    sp.dma_start(ep[:, par, i, 0:F], src).then_inc(ep_in[par], 16)
                sp.dma_start(ep[:, par, 2, 0:F + 1], ft_dram[t]).then_inc(ep_in[par], 16)

            def store_out(v, par):
                sp.wait_ge(S["out_done"], 2 * v + par + 1)
                sp.dma_start(out_t[2 * v + par], ep[:, par, 3, 0:F]).then_inc(o_out[par], 16)

            sp.wait_ge(S["tr_done"], GROUPS)
            sp.wait_ge(S["sq_done"], GROUPS // 2)
            for i in range(PAIR_SLOTS):
                sp.wait_ge(ut_out[i], 16 * GROUPS // PAIR_SLOTS)
            for q in range(QPT):
                load_fx(2 * q)
                if q < QPT - 1:
                    load_fx(2 * q + 1)
                load_ut(0, q, True)
            load_fx(NXG - 1)
            sp.wait_ge(S["mm_done"], GROUPS)
            load_ep(0, 0, True)
            for q in range(QPT, 2 * QPT):
                load_ut(0, q, True)
            load_ep(0, 1, True)
            with sp.Fori(1, PAIRS) as v:
                for par in range(2):
                    for q in range(QPT):
                        load_ut(v, par * QPT + q, False)
                    load_ep(v, par, False)
                    store_out(v - 1, par)
            for par in range(2):
                store_out(PAIRS - 1, par)
            for par in range(2):
                sp.wait_ge(o_out[par], 16 * PAIRS)

        @block.gpsimd
        def _(pool):
            pool.memset(ident[:, :], 0.0).then_inc(S["id_done"], 1)
            pool.wait_ge(S["id_done"], 1)
            pool.affine_select(out=ident[:, :], in_=ident[:, :], compare_op=ALU.not_equal, fill=1.0, base=0,
                               pattern=[[-1, P]], channel_multiplier=1).then_inc(S["id_done"], 1)
            pool.wait_ge(S["id_done"], 2)
            pool.tensor_scalar(neg_ident[:, :], ident[:, :], -1.0, None, ALU.mult).then_inc(S["id_done"], 1)
            pool.wait_ge(S["coef_chain"], 7)

            def wait(semaphore, value):
                pool.wait_ge(semaphore, value)
                pool.sem_inc(S["pool_waited"], 1)

            def epilogue(t, par, first):
                def then(op, i):
                    op.then_inc(S["pool_chain"], 1)
                    wait(S["pool_chain"], POOL_OPS * t + i)

                wait(S["sq_done"], CPT * (t + 1))
                then(pool.tensor_tensor(two_sq, sq_part[:, par, 0:2], sq_part[:, par, 2:4], ALU.add), 1)
                then(pool.tensor_tensor(sq_sum, two_sq[:, 0:1], two_sq[:, 1:2], ALU.add), 2)
                wait(S["hs_in"], 16 * (t + 1))
                then(pool.tensor_scalar(hrow[:, F:F + 1], sq_sum, 0.5, None, ALU.mult), 3)
                then(pool.tensor_scalar(s_row, hrow[:, F:F + 1], -1.0 / H_SCALE, m2s, ALU.mult, ALU.add), 4)
                then(pool.tensor_scalar(hrow[:, 0:F], hrow[:, 0:F], s_row, None, ALU.mult), 5)
                wait(S["pu_done"], t + 1)
                then(pool.tensor_tensor(hrow[:, 0:F], hrow[:, 0:F], pu[:, :], ALU.add), 6)
                then(pool.tensor_scalar(pu[:, :], hrow[:, 0:F], THRESH, -THRESH, ALU.min, ALU.max), 7)
                then(pool.tensor_tensor(hrow[:, 0:F], hrow[:, 0:F], pu[:, :], ALU.subtract), 8)
                then(pool.tensor_scalar(pu[:, :], hrow[:, 0:F], FEAT_SCALE, None, ALU.mult), 9)
                if not first:
                    wait(S["scratch_out"], HS_STORED + 32 * t)
                then(pool.tensor_copy(fpair[:, 0:F], pu[:, :]), 10)
                pool.tensor_tensor(fpair[:, F:2 * F], pu[:, :], fpair[:, 0:F], ALU.subtract)\
                    .then_inc(S["feat_done"], 1)

            epilogue(0, 0, True)
            epilogue(1, 1, False)
            with pool.Fori(1, PAIRS) as u:
                for par in range(2):
                    epilogue(2 * u + par, par, False)

        @block.scalar
        def _(act):
            act.dma_start(acol, a.rearrange("(w p) o -> p (w o)", p=P), allow_slow_non_contiguous=True)\
                .then_inc(S["acol_in"], 16)
            act.dma_start(sig, temp.partition_broadcast(P)).then_inc(S["temp_in"], 16)
            act.wait_ge(S["ve_done"], 1)
            act.activation(rstd, ve, ACT.Sqrt).then_inc(S["sd_done"], 1)
            act.wait_ge(S["nb_done"], 1)

            def f2_out(b):
                act.wait_ge(S["f2_ps"], b + 1)
                act.activation(row_q[:, b * BLK * P:(b + 1) * BLK * P], acc[b % 2][:, :], ACT.Copy,
                               scale=1.0 / H_SCALE).then_inc(S["f2_sb"], 1)

            for t in range(TILES):
                act.activation(xs[:, t, :], xs[:, t, :], ACT.Relu, bias=nbias[:, t:t + 1],
                               scale=hsc[:, t:t + 1]).then_inc(S["relu_done"], 1)
                if t % BLK == BLK - 1 and t >= 3 * BLK:
                    f2_out(t // BLK - 3)
            for b in range(NBLK - 3, NBLK):
                f2_out(b)
            act.wait_ge(S["gm_chain"], 4)
            act.wait_ge(S["f2_sb"], NBLK)
            for c in range(CPT):
                cs = slice(c * CHUNK, (c + 1) * CHUNK)
                act.activation(row_b[:, cs], row_q[:, cs], ACT.Exp, bias=ngmax).then_inc(S["row_done"], 1)
                act.wait_ge(S["row_done"], 2 * c + 1)
                act.activation(row_q[:, cs], row_q[:, cs], ACT.Exp, bias=ngmax_q, scale=ALPHA)\
                    .then_inc(S["row_done"], 1)
                if c == 0:
                    act.wait_ge(S["f1_done"], NBLK)
                    act.activation(c_all[:, :], ps_f1[:, :], ACT.Exp, bias=gmax_c,
                                   scale=(1.0 - ALPHA) / H_SCALE).then_inc(S["c_done"], 1)
            act.wait_ge(S["temp_in"], 16)
            act.activation(sig, sig, ACT.Exp, scale=-1.0).then_inc(S["sig_e"], 1)

            def high(u, k, first):
                act.wait_ge(S["tr_done"], STEPS * u + k + 1)
                if not (first and k < PAIR_SLOTS):
                    act.wait_ge(S["mm_done"], STEPS * u + k - PAIR_SLOTS + 1)
                    act.wait_ge(ut_out[k % PAIR_SLOTS],
                                16 * (STEPS // PAIR_SLOTS * u + k // PAIR_SLOTS))
                act.activation(pair[:, k % PAIR_SLOTS, 0, :], ps_t[k % 2][:, :], ACT.Copy).then_inc(S["hi_done"], 1)

            def step(u, k, first, fill):
                par, ck = (k // GPT) % 2, (k % GPT) // 2
                chunk = vbuf[:, par, ck * CHUNK:(ck + 1) * CHUNK]
                t, c = 2 * u + k // GPT, GPT * u + k // 2
                if fill and k % 2 == 0:
                    if k % GPT == 0:
                        act.wait_ge(S["r_done"], t + 1)
                    act.activation(chunk, chunk, ACT.Identity, bias=rbias[par], scale=rnorm[par])\
                        .then_inc(S["norm_done"], 1)
                if fill and k % 2 == 1:
                    act.wait_ge(S["norm_done"], c + 1)
                    if k % GPT == 1 and not first:
                        act.wait_ge(S["pool_chain"], POOL_OPS * (t - 2) + 1)
                    if not (first and k == 1):
                        act.wait_ge(S["sq_done"], c)
                    act.sem_inc(S["act_waited"], 1)
                    act.activation(junk[:, :], chunk, ACT.Square, scale=1.0 / U_SCALE, saturate=False,
                                   accum_out=sq_part[:, par, ck:ck + 1]).then_inc(S["sq_done"], 1)
                m = k - HI_LAG - 1
                if (not first or m >= 0) and m < STEPS and m % GPT in BY_SCALAR:
                    t = 2 * u + m // GPT
                    act.wait_ge(S["res_done"], len(BY_SCALAR) * t + BY_SCALAR.index(m % GPT) + 1)
                    act.activation(pair[:, m % PAIR_SLOTS, 1, :], ps_t[m % 2][:, :], ACT.Copy).then_inc(S["lo_s"], 1)
                if (not first or k >= HI_LAG) and k < STEPS + HI_LAG:
                    high(u, k - HI_LAG, first)
                s = k // GPT - 2
                if k % GPT == 0 and (not first or s >= 0):
                    t = 2 * u + s
                    act.wait_ge(S["feat_done"], t + 1)
                    act.dma_start(fh_dram[t], fpair[:, :]).then_inc(S["scratch_out"], 16)
                    act.dma_start(ft_dram[t], hrow[:, :]).then_inc(S["scratch_out"], 16)
                s = k // GPT - 1
                if k % GPT == E1_AT and s < 2 and (not first or s >= 0):
                    t = 2 * u + s
                    act.wait_ge(S["mm_done"], GPT * (t + 1))
                    if not (first and s == 0):
                        act.wait_ge(S["feat_done"], t)
                    act.activation(pu[:, :], acc[s % 2][:, F:2 * F], ACT.Copy,
                                   scale=1.0 / (U_SCALE * H_SCALE)).then_inc(S["e1_done"], 1)

            pairs(act, step, GPT + 1)

            def phase2(v, par):
                t = 2 * v + par
                act.wait_ge(S["mm2_done"], QPT * (t + 1))
                if not (isinstance(t, int) and t == 0):
                    act.wait_ge(S["out_done"], t)
                act.activation(pu[:, :], acc[par][:, F:2 * F], ACT.Copy,
                               scale=1.0 / (U_SCALE * FEAT_SCALE)).then_inc(S["e3_done"], 1)

            act.wait_ge(S["feat_done"], TILES)
            phase2(0, 0)
            phase2(0, 1)
            with act.Fori(1, PAIRS) as v:
                phase2(v, 0)
                phase2(v, 1)

        @block.vector
        def _(dve):
            dve.wait_ge(S["acol_in"], 16)
            for k in range(2):
                dve.tensor_copy(a2_wide[:, k, :], acol[:, 2 + k:3 + k].to_broadcast([P, P]))\
                    .then_inc(S["a2_done"], 1)
            for g in range(NXG):
                dve.wait_ge(x_in[g], 16)
                for t in range(g * XG, (g + 1) * XG):
                    dve.bn_stats(stats[:, t, :], xs[:, t, :]).then_inc(S["stats_done"], 1)
            dve.wait_ge(S["stats_done"], TILES)
            for t in range(TILES):
                dve.bn_aggr(mv[:, t, :], stats[:, t, :]).then_inc(S["aggr_done"], 1)
            dve.wait_ge(S["aggr_done"], TILES)
            dve.tensor_scalar(ve, mv[:, :, 1], EPS, None, ALU.add).then_inc(S["ve_done"], 1)
            dve.wait_ge(S["sd_done"], 1)
            done = [0]

            def then(name, op):
                done[0] += 1
                op.then_inc(S[name], 1)
                dve.wait_ge(S[name], done[0])

            then("rstd_chain", dve.reciprocal(rstd, rstd))
            then("rstd_chain", dve.tensor_tensor(ytmp, rstd, rstd, ALU.mult))
            then("rstd_chain", dve.tensor_tensor(ytmp, ytmp, ve, ALU.mult))
            then("rstd_chain", dve.tensor_scalar(ytmp, ytmp, -0.5 * H_SCALE, 1.5 * H_SCALE, ALU.mult, ALU.add))
            then("rstd_chain", dve.tensor_tensor(hsc, rstd, ytmp, ALU.mult))
            dve.scalar_tensor_tensor(nbias, mv[:, :, 0], -1.0, hsc, ALU.mult, ALU.mult).then_inc(S["nb_done"], 1)

            def split_h(b):
                ts = slice(b * BLK, (b + 1) * BLK)
                dve.wait_ge(S["relu_done"], BLK * (b + 1))
                dve.tensor_copy(xpair[:, ts, 0:F], xs[:, ts, :]).then_inc(S["split_done"], 1)
                dve.wait_ge(S["split_done"], 2 * b + 1)
                dve.tensor_tensor(xpair[:, ts, F:2 * F], xs[:, ts, :], xpair[:, ts, 0:F], ALU.subtract)\
                    .then_inc(S["split_done"], 1)

            for b in range(NBLK):
                dve.wait_ge(S["ht_ps"], b + 1)
                if b >= 2:
                    dve.wait_ge(S["f1_done"], b - 1)
                dve.tensor_copy(h_t[b % 2], ps_t[b % 2][:, :]).then_inc(S["ht_sb"], 1)
                split_h(b)
                if b >= 2:
                    dve.wait_ge(S["f2_sb"], b - 1)
                    dve.reduce_max(gblk[:, b - 2:b - 1], row_q[:, (b - 2) * BLK * P:(b - 1) * BLK * P], AX.X)\
                        .then_inc(S["blk_max"], 1)
            for b in range(NBLK - 2, NBLK):
                dve.wait_ge(S["f2_sb"], b + 1)
                dve.reduce_max(gblk[:, b:b + 1], row_q[:, b * BLK * P:(b + 1) * BLK * P], AX.X)\
                    .then_inc(S["blk_max"], 1)
            dve.wait_ge(S["blk_max"], NBLK)
            done[0] = 0
            then("gm_chain", dve.reduce_max(gmax, gblk, AX.X))
            then("gm_chain", dve.tensor_scalar(ngmax, gmax, -1.0, None, ALU.mult))
            then("gm_chain", dve.tensor_scalar(ngmax_q, gmax, -ALPHA, None, ALU.mult))
            then("gm_chain", dve.tensor_scalar(gmax_c, gmax, 1.0 - ALPHA, None, ALU.mult))
            dve.wait_ge(S["sig_e"], 1)
            done[0] = 0
            then("coef_chain", dve.tensor_scalar(sig, sig, 1.0, None, ALU.add))
            then("coef_chain", dve.reciprocal(sig, sig))
            then("coef_chain", dve.tensor_scalar(m2s, sig[:, 2:3], -1.0 / H_SCALE, 1.0 / H_SCALE, ALU.mult, ALU.add))
            then("coef_chain", dve.tensor_scalar(nc3, sig[:, 3:4], -1.0, None, ALU.mult))
            then("coef_chain", dve.tensor_copy(c1, sig[:, 1:2]))
            then("coef_chain", dve.tensor_scalar(om1, sig[:, 1:2], -1.0, 1.0, ALU.mult, ALU.add))
            then("coef_chain", dve.tensor_scalar(om0, sig[:, 0:1], -1.0, 1.0, ALU.mult, ALU.add))
            then("coef_chain", dve.tensor_tensor(k0, om1, om0, ALU.mult))
            then("coef_chain", dve.tensor_tensor(k_a, om1, sig[:, 0:1], ALU.mult))
            dve.wait_ge(S["c_done"], 1)
            dve.wait_ge(S["scratch_out"], 16 * NXG)

            def step(u, k, first, fill):
                par, g = (k // GPT) % 2, k % GPT
                t = 2 * u + k // GPT
                if fill and k % 2 == 0:
                    cs = slice(g * GROUP, g * GROUP + CHUNK)
                    if first:
                        if k < GPT:
                            dve.wait_ge(S["row_done"], g + 2)
                    else:
                        dve.wait_ge(S["tr_done"], STEPS * u + k - STEPS + 2)
                        dve.wait_ge(S["sq_done"], GPT * u + k // 2 - GPT + 1)
                    dve.scalar_tensor_tensor(vbuf[:, par, cs], row_b[:, cs], c_all[:, bass.ds(t, 1)],
                                             row_q[:, cs], ALU.mult, ALU.max).then_inc(S["t_done"], 1)
                    dve.wait_ge(S["t_done"], GPT * u + k // 2 + 1)
                if fill:
                    gs = slice(g * GROUP, (g + 1) * GROUP)
                    dve.wait_ge(adj_in[k % ADJ_SLOTS], 16 * (STEPS // ADJ_SLOTS * u + k // ADJ_SLOTS + 1))
                    dve.scalar_tensor_tensor(vbuf[:, par, gs], adj_sb[:, k % ADJ_SLOTS, :], 0.0, vbuf[:, par, gs],
                                             ALU.is_gt, ALU.mult, accum_out=vs[:, par, g:g + 1])\
                        .then_inc(S["v_done"], 1)
                if fill and g == GPT - 1:
                    chain = S["den_chain"]
                    dve.wait_ge(S["v_done"], STEPS * u + k + 1)
                    dve.reduce_sum(vsum, vs[:, par, :], AX.X).then_inc(chain, 1)
                    dve.wait_ge(chain, 3 * t + 1)
                    dve.tensor_scalar(rbias[par], vsum, 0.0, U_SCALE / N, ALU.is_equal, ALU.mult).then_inc(chain, 1)
                    dve.wait_ge(chain, 3 * t + 2)
                    dve.scalar_tensor_tensor(wden, vsum, 1.0 / U_SCALE, rbias[par], ALU.mult, ALU.add)\
                        .then_inc(chain, 1)
                    dve.wait_ge(chain, 3 * t + 3)
                    dve.reciprocal(rnorm[par], wden).then_inc(S["r_done"], 1)
                m = k - SPLIT_LAG
                if (not first or m >= 0) and m % GPT not in BY_SCALAR:
                    dve.wait_ge(S["hi_done"], STEPS * u + m + 1)
                    dve.tensor_tensor(pair[:, m % PAIR_SLOTS, 1, :], ps_t[m % 2][:, :], pair[:, m % PAIR_SLOTS, 0, :],
                                      ALU.subtract)\
                        .then_inc(S["lo_v"], 1)
                s = k // GPT - 2
                if g == E2_AT and (not first or s >= 0):
                    finish_pu(2 * u + s, s % 2, U_SCALE * H_SCALE, "e1_done", "pu_done")

            def finish_pu(t, par, scale, ready, done_name):
                dve.wait_ge(S[ready], t + 1)
                dve.scalar_tensor_tensor(pu[:, :], acc[par][:, 0:F], 1.0 / scale, pu[:, :], ALU.mult, ALU.add)\
                    .then_inc(S[done_name], 1)

            pairs(dve, step, SPLIT_LAG)
            finish_pu(TILES - 1, 1, U_SCALE * H_SCALE, "e1_done", "pu_done")

            def phase2(v, par, first):
                t = 2 * v + par
                xt, h0t, ft, o = (ep[:, par, i, 0:F] for i in range(4))
                rowsum = ep[:, par, 2, F:F + 1]
                chain = S["out_chain"]

                def then(op, i):
                    op.then_inc(chain, 1)
                    dve.wait_ge(chain, 5 * t + i)

                dve.wait_ge(ep_in[par], 48 * (v + 1))
                then(dve.scalar_tensor_tensor(k_i, rowsum, c1, k_a, ALU.mult, ALU.add), 1)
                dve.wait_ge(S["e3_done"], t + 1)
                then(dve.scalar_tensor_tensor(pu[:, :], acc[par][:, 0:F], 1.0 / (U_SCALE * FEAT_SCALE), pu[:, :],
                                              ALU.mult, ALU.add), 2)
                if not first:
                    dve.wait_ge(o_out[par], 16 * v)
                then(dve.scalar_tensor_tensor(ft, pu[:, :], nc3, ft, ALU.mult, ALU.add), 3)
                then(dve.scalar_tensor_tensor(o, pu[:, :], c1, xt, ALU.mult, ALU.add), 4)
                then(dve.scalar_tensor_tensor(o, ft, k_i, o, ALU.mult, ALU.add), 5)
                dve.scalar_tensor_tensor(o, h0t, k0, o, ALU.mult, ALU.add).then_inc(S["out_done"], 1)

            phase2(0, 0, True)
            phase2(0, 1, True)
            with dve.Fori(1, PAIRS) as v:
                phase2(v, 0, False)
                phase2(v, 1, False)

        @block.tensor
        def _(pe):
            pe.wait_ge(S["id_done"], 2)
            pe.wait_ge(S["a2_done"], 2)
            pe.wait_ge(S["id_done"], 3)

            def f2_block(b):
                pe.wait_ge(S["ht_sb"], b + 1)
                if b >= 2:
                    pe.wait_ge(S["f2_sb"], b - 1)
                for k in range(2):
                    last = pe.matmul(acc[b % 2][:, :], a2_wide[:, k, :], h_t[b % 2][:, k * BLK * P:(k + 1) * BLK * P],
                                     start=(k == 0), stop=(k == 1))
                last.then_inc(S["f2_ps"], 1)
                for i in range(BLK):
                    for k in range(2):
                        c0 = (k * BLK + i) * P
                        last = pe.matmul(ps_f1[:, b * BLK + i:b * BLK + i + 1], h_t[b % 2][:, c0:c0 + P],
                                         acol[:, k:k + 1], start=(k == 0), stop=(k == 1))
                last.then_inc(S["f1_done"], 1)

            for b in range(NBLK):
                pe.wait_ge(S["relu_done"], BLK * (b + 1))
                if b >= 2:
                    pe.wait_ge(S["ht_sb"], b - 1)
                for k in range(2):
                    for i in range(BLK):
                        c0 = (k * BLK + i) * P
                        last = pe.transpose(ps_t[b % 2][:, c0:c0 + P], xs[:, b * BLK + i, k * P:(k + 1) * P], ident[:, :])
                last.then_inc(S["ht_ps"], 1)
                if b >= 1:
                    f2_block(b - 1)
            f2_block(NBLK - 1)
            pe.wait_ge(S["c_done"], 1)
            pe.wait_ge(S["split_done"], 2 * NBLK)

            def products(par, high, low, feats, start, stop):
                whole = lambda stop: pe.matmul(acc[par][:, :], high, feats, start=start, stop=stop)
                half = lambda: pe.matmul(acc[par][:, 0:F], low, feats[:, 0:F], start=False, stop=False)
                if stop:
                    half()
                    return whole(True)
                whole(False)
                return half()

            def step(u, k, first, fill):
                par, g = (k // GPT) % 2, k % GPT
                if fill:
                    if k % 2 == 0:
                        pe.wait_ge(S["norm_done"], GPT * u + k // 2 + 1)
                    if not (first and k < 2):
                        wait_lo(pe, u, k - 2)
                    for q in range(QPG):
                        c0 = g * GROUP + q * P
                        last = pe.matmul(ps_t[k % 2][:, q * P:(q + 1) * P], vbuf[:, par, c0:c0 + P], ident[:, :],
                                         is_transpose=True, start=(q % 4 == 0), stop=(q % 4 == 3))
                    last.then_inc(S["tr_done"], 1)
                m = k - 1
                if (not first or m >= 0) and m < STEPS and m % GPT in BY_SCALAR:
                    pe.wait_ge(S["hi_done"], STEPS * u + m + 1)
                    for q in range(2):
                        qs = slice(q * 4 * P, (q + 1) * 4 * P)
                        last = pe.matmul(ps_t[m % 2][:, qs], neg_ident[:, :], pair[:, m % PAIR_SLOTS, 0, qs],
                                         start=False, stop=True, skip_group_check=True)
                    last.then_inc(S["res_done"], 1)
                m = k - MM_LAG
                if not first or m >= 0:
                    par, g = (m // GPT) % 2, m % GPT
                    t = 2 * u + m // GPT
                    wait_lo(pe, u, m)
                    if g == 0 and not (first and m < STEPS):
                        pe.wait_ge(S["pu_done"], t - 1)
                    for q in range(QPG):
                        j = g * QPG + q
                        last = products(par, pair[:, m % PAIR_SLOTS, 0, q * P:(q + 1) * P],
                                        pair[:, m % PAIR_SLOTS, 1, q * P:(q + 1) * P], xpair[:, j, :], j == 0, j == TILES - 1)
                    last.then_inc(S["mm_done"], 1)

            pairs(pe, step, MM_LAG)

            def phase2(v, par, first):
                t = 2 * v + par
                for q in range(QPT):
                    slot = par * QPT + q
                    if first and par == 0:
                        pe.wait_ge(fx_in[2 * q], 16)
                        pe.wait_ge(fx_in[2 * q + 1], 16)
                    if q == 0:
                        if first:
                            pe.wait_ge(S["pu_done"], TILES - 1 + par)
                        else:
                            pe.wait_ge(S["out_done"], t - 1)
                    pe.wait_ge(ut_in[slot], 16 * (v + 1))
                    for i in range(2 * QPG):
                        j = q * 2 * QPG + i
                        c0 = (i // QPG) * 2 * GROUP + (i % QPG) * P
                        last = products(par, ut_sb[:, slot, c0:c0 + P], ut_sb[:, slot, c0 + GROUP:c0 + GROUP + P],
                                        fx[:, j, :], j == 0, j == TILES - 1)
                    last.then_inc(S["mm2_done"], 1)

            phase2(0, 0, True)
            phase2(0, 1, True)
            with pe.Fori(1, PAIRS) as v:
                phase2(v, 0, False)
                phase2(v, 1, False)


def kernel(x, adj, L0_gnn_h0, L0_gnn_a, L0_gnn_temp):
    import numpy as _np
    import concourse.bacc as _bacc
    from concourse import mybir as _mybir
    from concourse.bass_utils import run_bass_kernel_spmd as _run

    nc = _bacc.Bacc("TRN2", target_bir_lowering=False, num_devices=1, dynamic_dma_scratch_size=1024)
    given = {"x": x, "adj": adj, "h0": L0_gnn_h0, "a": L0_gnn_a, "temp": L0_gnn_temp}
    arrays, args = {}, []
    for name, value in given.items():
        v = _np.ascontiguousarray(value)
        arrays[f"in_{name}"] = v
        args.append(nc.dram_tensor(f"in_{name}", v.shape, _mybir.dt.from_np(v.dtype), kind="ExternalInput").ap())
    out = nc.dram_tensor("out_0", x.shape, _mybir.dt.float32, kind="ExternalOutput").ap()
    graph_attention_layer(nc, *args, out)
    r = _run(nc, [arrays], core_ids=[0])
    return r.results[0]["out_0"]
```

```python
import concourse.bass as bass
from concourse import mybir
from contextlib import ExitStack


def graph_attention_layer(nc, x, adj, h0, a, temp, out):
    F32, F16, BF16 = mybir.dt.float32, mybir.dt.float16, mybir.dt.bfloat16
    ALU = mybir.AluOpType
    ACT = mybir.ActivationFunctionType
    AX = mybir.AxisListType

    P = 128
    N, F = x.shape
    TILES = N // P
    GROUP = 1024
    GPT = N // GROUP
    QPG = GROUP // P
    BODY = 3
    STEPS = BODY * GPT
    TURNS = TILES // BODY
    END = TILES * GPT - (TURNS - 1) * STEPS
    V_SLOTS = 12
    GROUPS = TILES * GPT
    CHUNK = 2 * GROUP
    CPT = N // CHUNK
    ADJ_SLOTS = 4
    PAIR_SLOTS = 4
    XG = 8
    NXG = TILES // XG
    BLK = 4
    NBLK = TILES // BLK
    F2_LAG = 2
    F1_LAG = 2
    MAX_LAG = 2
    HT_BY_SCALAR = 6
    EARLY = 2
    SD_AT = 23
    HALF = TILES // 2

    ALPHA, EPS, THRESH = 0.2, 1e-5, 1e-6
    H_SCALE = 2.0 ** 11
    U_SCALE = 2.0 ** 15
    FEAT_SCALE = 2.0 ** 10

    C_MAX = 3.7e32

    HI_LAG = 2
    SPLIT_LAG = GPT + 3
    STORE_LAG = SPLIT_LAG + 3
    BY_SCALAR = (3,)
    E1_AT, E2_AT = 5, 6
    FX_AT, UT_AT = 5, 9
    MM_LAG = 2

    hs_dram = nc.dram_tensor("hs_scratch", (TILES, P, F), F32, kind="Internal").ap()
    ut_dram = nc.dram_tensor("ut_scratch", (TILES * GPT, P, 2 * GROUP), F16, kind="Internal").ap()
    fh_dram = nc.dram_tensor("feat_pair_scratch", (TILES, P, 2 * F), F16, kind="Internal").ap()
    ft_dram = nc.dram_tensor("feat_scratch", (TILES, P, F + 1), F32, kind="Internal").ap()
    x_t = x.rearrange("(t p) f -> t p f", p=P)
    h0_t = h0.rearrange("(t p) f -> t p f", p=P)
    out_t = out.rearrange("(t p) f -> t p f", p=P)
    adj_t = adj.rearrange("(t p) (g c) -> t g p c", p=P, c=GROUP)

    ctx = ExitStack()
    with ctx:
        def sb(name, shape, dt=F32):
            return ctx.enter_context(nc.sbuf_tensor(name, shape, dt))

        def pb(name, shape):
            return ctx.enter_context(nc.psum_tensor(name, shape, F32))

        def sem(name):
            return ctx.enter_context(nc.semaphore(name))

        rows = sb("rows", [P, 2, N])
        row_b, row_q = rows[:, 0, :], rows[:, 1, :]
        work = sb("work", [P, V_SLOTS + ADJ_SLOTS, GROUP])
        adj_sb = work[:, V_SLOTS:V_SLOTS + ADJ_SLOTS, :]
        xpair = sb("xpair", [P, TILES, 2 * F], F16)
        pair = sb("pair", [P, PAIR_SLOTS, 2, GROUP], F16)
        junk = sb("junk", [P, CHUNK], BF16)
        pu = sb("pu", [P, F])
        hrow = sb("hrow", [P, F + 1])
        fpair = sb("fpair", [P, 2 * F], F16)
        ident = sb("ident", [P, P])
        neg_ident = sb("neg_ident", [P, P], F16)
        c_all = sb("c_all", [P, TILES])
        vs = sb("vs", [P, BODY, GPT])
        sq_part = sb("sq_part", [P, BODY, CPT])
        small = sb("small", [P, 40])
        vsum, wden = small[:, 0:1], small[:, 1:2]
        rnorm = [small[:, 32 + i:33 + i] for i in range(BODY)]
        rbias = [small[:, 35 + i:36 + i] for i in range(BODY)]
        two_sq, s_row = small[:, 6:8], small[:, 8:9]
        gmax, ngmax, ngmax_q, gmax_c = (small[:, 9 + i:10 + i] for i in range(4))
        sig = small[:, 13:18]
        c1, nc3, m2s, k0, k_a, k_i = (small[:, 18 + i:19 + i] for i in range(6))
        om1, om0 = small[:, 24:25], small[:, 25:26]
        sq_sum = small[:, 26:27]
        acol = small[:, 28:32]

        acc = [pb(f"acc{i}", [P, 2 * F]) for i in range(BODY)]
        ps_t = [pb(f"ps_t{i}", [P, GROUP]) for i in range(2)]
        ps_f1 = pb("ps_f1", [P, TILES])
        gmax_ps = acc[2][:, 0:1]

        xs = work[:, :, :].rearrange("p a (t f) -> p (a t) f", f=F)
        stats = row_b[:, 0:TILES * 6].rearrange("p (t s) -> p t s", s=6)
        mv = row_b[:, TILES * 6:TILES * 8].rearrange("p (t s) -> p t s", s=2)
        ve, rstd, ytmp, hsc, nbias = (row_b[:, TILES * (8 + i):TILES * (9 + i)] for i in range(5))
        gblk = pu[:, 0:NBLK]
        one = ident[0:1, 0:1]
        h_t = [pair[:, i, :, :].rearrange("p a c -> p (a c)").bitcast(F32) for i in range(2)]
        a2_wide = hrow[:, 0:F].rearrange("p (k m) -> p k m", m=P)
        fx = rows[:, :, :].rearrange("p a n -> p (a n)").bitcast(F16).rearrange("p (t f) -> p t f", f=2 * F)
        ut_sb = work[:, :, :].rearrange("p a n -> p (a n)").bitcast(F16).rearrange("p (s c) -> p s c", c=4 * GROUP)
        ep = pair[:, :, :, :].rearrange("p s a c -> p (s a c)").bitcast(F32)[:, 0:8 * (F + 4)].rearrange(
            "p (s k f) -> p s k f", s=2, f=F + 4)

        names = """id_done acol_in temp_in a2_done stats_done aggr_done ve_done sd_done rstd_chain nb_done relu_done
            h_hi h_lo ht_ps ht_a ht_v f2_ps f2_sb f1_done blk_max gm_ps gm_chain row0_first row0_last row_done c_done c_capped
            sig_e coef_chain scratch_out t_done v_done den_chain r_done norm_done sq_done tr_done hi_done
            res_done lo_v lo_s mm_done e1_done pu_done pool_waited pool_chain feat_done hs_in
            mm2_done e3_done out_chain out_done""".split()
        S = {n: sem(n) for n in names}
        x_in = [sem(f"x_in{i}") for i in range(NXG)]
        adj_in = [sem(f"adj_in{i}") for i in range(ADJ_SLOTS)]
        ut_out = [sem(f"ut_out{i}") for i in range(PAIR_SLOTS)]
        PAIRS = TILES // 2
        UT_SLOTS = 8
        QPT = GPT // 2
        ut_in = [sem(f"ut_in{i}") for i in range(UT_SLOTS)]
        fx_in = [sem(f"fx_in{i}") for i in range(NXG)]
        ep_in = [sem(f"ep_in{i}") for i in range(2)]
        o_out = [sem(f"o_out{i}") for i in range(2)]

        def wait_ht(eng, b):
            if b < HT_BY_SCALAR:
                eng.wait_ge(S["ht_a"], b + 1)
            else:
                eng.wait_ge(S["ht_v"], b - HT_BY_SCALAR + 1)

        def wait_lo(eng, u, m):
            t, g = BODY * u + m // GPT, m % GPT
            by_s = [i for i in range(g + 1) if i in BY_SCALAR]
            if g in BY_SCALAR:
                eng.wait_ge(S["lo_s"], len(BY_SCALAR) * t + len(by_s))
            else:
                eng.wait_ge(S["lo_v"], (GPT - len(BY_SCALAR)) * t + g + 1 - len(by_s))

        HS_STORED = 16 * NXG
        POOL_OPS = 10

        def turns(eng, step, lag):
            for k in range(STEPS):
                step(0, k, True)
            with eng.Fori(1, TURNS) as u:
                for k in range(STEPS):
                    step(u, k, False)
            for k in range(STEPS, END + lag):
                step(TURNS - 1, k, False)

        def exists(m, first):
            return (m >= 0 or not first) and m < END

        block = ctx.enter_context(nc.Block())

        @block.sync
        def _(sp):
            for g in range(NXG):
                sp.dma_start(xs[:, g * XG:(g + 1) * XG, :],
                             x_t[g * XG:(g + 1) * XG].rearrange("t p f -> p t f")).then_inc(x_in[g], 16)
            for g in range(NXG):
                sp.wait_ge(S["relu_done"], XG * (g + 1))
                sp.dma_start(hs_dram[g * XG:(g + 1) * XG].rearrange("t p f -> p t f"),
                             xs[:, g * XG:(g + 1) * XG, :]).then_inc(S["scratch_out"], 16)
            sp.wait_ge(S["scratch_out"], HS_STORED)
            sp.wait_ge(S["h_lo"], NBLK)
            sp.wait_ge(S["ht_ps"], NBLK)
            for g in range(ADJ_SLOTS):
                sp.dma_start(adj_sb[:, g, :], adj_t[0, g]).then_inc(adj_in[g], 16)

            def load_fx(g):
                sp.wait_ge(S["scratch_out"], HS_STORED + 32 * XG * (g + 1))
                sp.dma_start(fx[:, g * XG:(g + 1) * XG, :],
                             fh_dram[g * XG:(g + 1) * XG].rearrange("t p f -> p t f")).then_inc(fx_in[g], 16)

            def load_ut(v, q, first):
                if not first:
                    sp.wait_ge(S["mm2_done"], UT_SLOTS * v + q - UT_SLOTS + 1)
                sp.dma_start(ut_sb[:, q, :].rearrange("p (g c) -> p g c", g=2),
                             ut_dram[bass.ds(2 * GPT * v + 2 * q, 2)].rearrange("g p c -> p g c"))\
                    .then_inc(ut_in[q], 16)

            def load_ep(v, par, first):
                t = 2 * v + par
                if not first:
                    sp.wait_ge(S["out_done"], t - 1)
                for i, src in enumerate((x_t[t], h0_t[t])):
                    sp.dma_start(ep[:, par, i, 0:F], src).then_inc(ep_in[par], 16)
                sp.dma_start(ep[:, par, 2, 0:F + 1], ft_dram[t]).then_inc(ep_in[par], 16)

            def store_out(v, par):
                sp.wait_ge(S["out_done"], 2 * v + par + 1)
                sp.dma_start(out_t[2 * v + par], ep[:, par, 3, 0:F]).then_inc(o_out[par], 16)

            def step(u, k, first):
                if k < END and not (first and k < ADJ_SLOTS):
                    sp.wait_ge(S["v_done"], STEPS * u + k - ADJ_SLOTS + 1)
                    sp.dma_start(adj_sb[:, k % ADJ_SLOTS, :], adj_t[BODY * u + k // GPT, k % GPT])\
                        .then_inc(adj_in[k % ADJ_SLOTS], 16)
                m = k - STORE_LAG
                if exists(m, first):
                    wait_lo(sp, u, m)
                    sp.dma_start(ut_dram[STEPS * u + m], pair[:, m % PAIR_SLOTS].rearrange("p a c -> p (a c)"))\
                        .then_inc(ut_out[m % PAIR_SLOTS], 16)
                m = k - 2 * GPT
                if exists(m, first) and k % GPT == 3:
                    t = BODY * u + m // GPT
                    sp.wait_ge(S["scratch_out"], HS_STORED + 32 * t)
                    sp.dma_start(hrow[:, 0:F], hs_dram[t]).then_inc(S["hs_in"], 16)

                e = k - END - FX_AT
                if e == 0:
                    sp.wait_ge(S["t_done"], GROUPS // 2)
                if 0 <= e < NXG - 1:
                    load_fx(e)
                e = k - END - UT_AT
                if e >= 0 and e % 2 == 0 and e // 2 < QPT:
                    q = e // 2
                    last_group = GROUPS - GPT + 2 * q + 2
                    sp.wait_ge(S["tr_done"], last_group)
                    sp.wait_ge(S["sq_done"], last_group // 2)
                    load_ut(0, q, True)

            turns(sp, step, 2 * GPT)

            sp.wait_ge(S["tr_done"], GROUPS)
            sp.wait_ge(S["sq_done"], GROUPS // 2)
            for i in range(PAIR_SLOTS):
                sp.wait_ge(ut_out[i], 16 * GROUPS // PAIR_SLOTS)
            load_fx(NXG - 1)
            sp.wait_ge(S["mm_done"], GROUPS)
            load_ep(0, 0, True)
            for q in range(QPT, 2 * QPT):
                load_ut(0, q, True)
            load_ep(0, 1, True)
            with sp.Fori(1, PAIRS) as v:
                for par in range(2):
                    for q in range(QPT):
                        load_ut(v, par * QPT + q, False)
                    load_ep(v, par, False)
                    store_out(v - 1, par)
            for par in range(2):
                store_out(PAIRS - 1, par)
            for par in range(2):
                sp.wait_ge(o_out[par], 16 * PAIRS)

        @block.gpsimd
        def _(pool):
            pool.memset(ident[:, :], 0.0).then_inc(S["id_done"], 1)
            pool.wait_ge(S["id_done"], 1)
            pool.affine_select(out=ident[:, :], in_=ident[:, :], compare_op=ALU.not_equal, fill=1.0, base=0,
                               pattern=[[-1, P]], channel_multiplier=1).then_inc(S["id_done"], 1)
            pool.wait_ge(S["id_done"], 2)
            pool.tensor_scalar(neg_ident[:, :], ident[:, :], -1.0, None, ALU.mult).then_inc(S["id_done"], 1)
            for b in range(NBLK):
                ts = slice(b * BLK, (b + 1) * BLK)
                pool.wait_ge(S["h_hi"], b + 1)
                pool.tensor_tensor(xpair[:, ts, F:2 * F], xs[:, ts, :], xpair[:, ts, 0:F], ALU.subtract)\
                    .then_inc(S["h_lo"], 1)
            pool.wait_ge(S["coef_chain"], 7)

            def wait(semaphore, value):
                pool.wait_ge(semaphore, value)
                pool.sem_inc(S["pool_waited"], 1)

            def epilogue(t, par, first):
                def then(op, i):
                    op.then_inc(S["pool_chain"], 1)
                    wait(S["pool_chain"], POOL_OPS * t + i)

                wait(S["sq_done"], CPT * (t + 1))
                then(pool.tensor_tensor(two_sq, sq_part[:, par, 0:2], sq_part[:, par, 2:4], ALU.add), 1)
                then(pool.tensor_tensor(sq_sum, two_sq[:, 0:1], two_sq[:, 1:2], ALU.add), 2)
                wait(S["hs_in"], 16 * (t + 1))
                then(pool.tensor_scalar(hrow[:, F:F + 1], sq_sum, 0.5, None, ALU.mult), 3)
                then(pool.tensor_scalar(s_row, hrow[:, F:F + 1], -1.0 / H_SCALE, m2s, ALU.mult, ALU.add), 4)
                then(pool.tensor_scalar(hrow[:, 0:F], hrow[:, 0:F], s_row, None, ALU.mult), 5)
                wait(S["pu_done"], t + 1)
                then(pool.tensor_tensor(hrow[:, 0:F], hrow[:, 0:F], pu[:, :], ALU.add), 6)
                then(pool.tensor_scalar(pu[:, :], hrow[:, 0:F], THRESH, -THRESH, ALU.min, ALU.max), 7)
                then(pool.tensor_tensor(hrow[:, 0:F], hrow[:, 0:F], pu[:, :], ALU.subtract), 8)
                then(pool.tensor_scalar(pu[:, :], hrow[:, 0:F], FEAT_SCALE, None, ALU.mult), 9)
                if not first:
                    wait(S["scratch_out"], HS_STORED + 32 * t)
                then(pool.tensor_copy(fpair[:, 0:F], pu[:, :]), 10)
                pool.tensor_tensor(fpair[:, F:2 * F], pu[:, :], fpair[:, 0:F], ALU.subtract)\
                    .then_inc(S["feat_done"], 1)

            for t in range(BODY):
                epilogue(t, t, t == 0)
            with pool.Fori(1, TURNS) as u:
                for par in range(BODY):
                    epilogue(BODY * u + par, par, False)
            epilogue(TILES - 1, (TILES - 1) % BODY, False)

        @block.scalar
        def _(act):
            act.dma_start(acol, a.rearrange("(w p) o -> p (w o)", p=P), allow_slow_non_contiguous=True)\
                .then_inc(S["acol_in"], 16)
            act.dma_start(sig, temp.partition_broadcast(P)).then_inc(S["temp_in"], 16)
            act.wait_ge(S["ve_done"], 1)
            act.activation(rstd[:, 0:HALF], ve[:, 0:HALF], ACT.Sqrt).then_inc(S["sd_done"], 1)

            def f2_out(b):
                act.wait_ge(S["f2_ps"], b + 1)
                act.activation(row_q[:, b * BLK * P:(b + 1) * BLK * P], acc[b % 2][:, :], ACT.Copy,
                               scale=1.0 / H_SCALE).then_inc(S["f2_sb"], 1)

            def fix_row0(b0, b1, done):
                act.wait_ge(S["f1_done"], b1)
                act.wait_ge(S["blk_max"], b1)
                cs = slice(b0 * BLK * P, b1 * BLK * P)
                act.dma_start(row_q[0:1, cs], row_q[1:2, cs]).then_inc(S[done], 16)

            for b in range(NBLK + F2_LAG):
                if b < NBLK:
                    for t in range(b * BLK, (b + 1) * BLK):
                        if t % HALF == 0:
                            act.wait_ge(S["nb_done"], t // HALF + 1)
                        act.activation(xs[:, t, :], xs[:, t, :], ACT.Relu, bias=nbias[:, t:t + 1],
                                       scale=hsc[:, t:t + 1]).then_inc(S["relu_done"], 1)
                        if t == SD_AT:
                            act.wait_ge(S["ve_done"], 2)
                            act.activation(rstd[:, HALF:TILES], ve[:, HALF:TILES], ACT.Sqrt)\
                                .then_inc(S["sd_done"], 1)
                if b == NBLK:
                    act.wait_ge(S["temp_in"], 16)
                    act.activation(sig, sig, ACT.Exp, scale=-1.0).then_inc(S["sig_e"], 1)
                if 1 <= b <= HT_BY_SCALAR:
                    act.wait_ge(S["ht_ps"], b)
                    if b >= 3:
                        act.wait_ge(S["f2_ps"], b - 2)
                    act.activation(h_t[(b - 1) % 2], ps_t[(b - 1) % 2][:, :], ACT.Copy).then_inc(S["ht_a"], 1)
                if b >= F2_LAG:
                    f2_out(b - F2_LAG)
                if b == NBLK + F2_LAG - 2:
                    fix_row0(0, NBLK * (CPT - 1) // CPT, "row0_first")
            act.wait_ge(S["gm_chain"], 4)
            act.wait_ge(S["f2_sb"], NBLK)
            act.activation(c_all[:, :], ps_f1[:, :], ACT.Exp, bias=gmax_c, scale=1.0 - ALPHA).then_inc(S["c_done"], 1)
            for c in range(CPT):
                cs = slice(c * CHUNK, (c + 1) * CHUNK)
                if c == 0:
                    act.wait_ge(S["row0_first"], 16)
                if c == CPT - 1:
                    act.wait_ge(S["row0_last"], 16)
                if c == 1:
                    fix_row0(NBLK * (CPT - 1) // CPT, NBLK, "row0_last")
                act.activation(row_b[:, cs], row_q[:, cs], ACT.Exp, bias=ngmax).then_inc(S["row_done"], 1)
                act.wait_ge(S["row_done"], 2 * c + 1)
                act.activation(row_q[:, cs], row_q[:, cs], ACT.Exp, bias=ngmax_q, scale=ALPHA)\
                    .then_inc(S["row_done"], 1)

            def high(u, k, first):
                act.wait_ge(S["tr_done"], STEPS * u + k + 1)
                if not (first and k < PAIR_SLOTS):
                    act.wait_ge(S["mm_done"], STEPS * u + k - PAIR_SLOTS + 1)
                    act.wait_ge(ut_out[k % PAIR_SLOTS],
                                16 * (STEPS // PAIR_SLOTS * u + k // PAIR_SLOTS))
                act.activation(pair[:, k % PAIR_SLOTS, 0, :], ps_t[k % 2][:, :], ACT.Copy).then_inc(S["hi_done"], 1)

            def step(u, k, first):
                par, ck = (k // GPT) % BODY, (k % GPT) // 2
                s0 = k // 2 * 2 % V_SLOTS
                chunk = work[:, s0:s0 + 2, :].rearrange("p a c -> p (a c)")
                t, c = BODY * u + k // GPT, STEPS // 2 * u + k // 2
                if k < END and k % 2 == 0:
                    if k % GPT == 0:
                        act.wait_ge(S["r_done"], t + 1)
                    act.activation(chunk, chunk, ACT.Identity, bias=rbias[par], scale=rnorm[par])\
                        .then_inc(S["norm_done"], 1)
                if k < END and k % 2 == 1:
                    act.wait_ge(S["norm_done"], c + 1)
                    if k % GPT == 1 and not (first and k < BODY * GPT):
                        act.wait_ge(S["pool_chain"], POOL_OPS * (t - BODY) + 1)
                    if not (first and k == 1):
                        act.wait_ge(S["sq_done"], c)
                    act.activation(junk[:, :], chunk, ACT.Square, scale=1.0 / U_SCALE,
                                   accum_out=sq_part[:, par, ck:ck + 1]).then_inc(S["sq_done"], 1)
                m = k - HI_LAG - 1
                if exists(m, first) and m % GPT in BY_SCALAR:
                    act.wait_ge(S["res_done"], len(BY_SCALAR) * (BODY * u + m // GPT) + BY_SCALAR.index(m % GPT) + 1)
                    act.activation(pair[:, m % PAIR_SLOTS, 1, :], ps_t[m % 2][:, :], ACT.Copy).then_inc(S["lo_s"], 1)
                m = k - HI_LAG
                if exists(m, first):
                    high(u, m, first)
                m = k - 2 * GPT
                if exists(m, first) and k % GPT == 0:
                    t = BODY * u + m // GPT
                    act.wait_ge(S["feat_done"], t + 1)
                    act.dma_start(fh_dram[t], fpair[:, :]).then_inc(S["scratch_out"], 16)
                    act.dma_start(ft_dram[t], hrow[:, :]).then_inc(S["scratch_out"], 16)
                m = k - GPT
                if exists(m, first) and k % GPT == E1_AT:
                    t = BODY * u + m // GPT
                    act.wait_ge(S["mm_done"], GPT * (t + 1))
                    if not (first and t == 0):
                        act.wait_ge(S["feat_done"], t)
                    act.activation(pu[:, :], acc[m // GPT % BODY][:, F:2 * F], ACT.Copy,
                                   scale=1.0 / (U_SCALE * H_SCALE)).then_inc(S["e1_done"], 1)

            turns(act, step, GPT + 1)

            def phase2(v, par):
                t = 2 * v + par
                act.wait_ge(S["mm2_done"], QPT * (t + 1))
                if not (isinstance(t, int) and t == 0):
                    act.wait_ge(S["out_done"], t)
                act.activation(pu[:, :], acc[1 + par][:, F:2 * F], ACT.Copy,
                               scale=1.0 / (U_SCALE * FEAT_SCALE)).then_inc(S["e3_done"], 1)

            act.wait_ge(S["feat_done"], TILES)
            phase2(0, 0)
            phase2(0, 1)
            with act.Fori(1, PAIRS) as v:
                phase2(v, 0)
                phase2(v, 1)

        @block.vector
        def _(dve):
            dve.wait_ge(S["acol_in"], 16)
            for k in range(2):
                dve.tensor_copy(a2_wide[:, k, 1:P], acol[:, 2 + k:3 + k].to_broadcast([P, P - 1]))\
                    .then_inc(S["a2_done"], 1)
                dve.tensor_copy(a2_wide[:, k, 0:1], acol[:, k:k + 1]).then_inc(S["a2_done"], 1)

            def layernorm_stats(g):
                ts = range(g * XG, (g + 1) * XG)
                dve.wait_ge(x_in[g], 16)
                for t in ts:
                    dve.bn_stats(stats[:, t, :], xs[:, t, :]).then_inc(S["stats_done"], 1)
                dve.wait_ge(S["stats_done"], XG * (g + 1))
                for t in ts:
                    dve.bn_aggr(mv[:, t, :], stats[:, t, :]).then_inc(S["aggr_done"], 1)

            def layernorm_scales(half):
                ts = slice(half * HALF, (half + 1) * HALF)
                chain = S["rstd_chain"]

                def then(op, i):
                    op.then_inc(chain, 1)
                    dve.wait_ge(chain, 5 * half + i)

                dve.wait_ge(S["sd_done"], half + 1)
                then(dve.reciprocal(rstd[:, ts], rstd[:, ts]), 1)
                then(dve.tensor_tensor(ytmp[:, ts], rstd[:, ts], rstd[:, ts], ALU.mult), 2)
                then(dve.tensor_tensor(ytmp[:, ts], ytmp[:, ts], ve[:, ts], ALU.mult), 3)
                then(dve.tensor_scalar(ytmp[:, ts], ytmp[:, ts], -0.5 * H_SCALE, 1.5 * H_SCALE, ALU.mult, ALU.add), 4)
                then(dve.tensor_tensor(hsc[:, ts], rstd[:, ts], ytmp[:, ts], ALU.mult), 5)
                dve.scalar_tensor_tensor(nbias[:, ts], mv[:, ts, 0], -1.0, hsc[:, ts], ALU.mult, ALU.mult)\
                    .then_inc(S["nb_done"], 1)

            def variances(half):
                ts = slice(half * HALF, (half + 1) * HALF)
                dve.wait_ge(S["aggr_done"], HALF * (half + 1))
                dve.tensor_scalar(ve[:, ts], mv[:, ts, 1], EPS, None, ALU.add).then_inc(S["ve_done"], 1)

            def block_max(b):
                dve.wait_ge(S["f2_sb"], b + 1)
                dve.reduce_max(gblk[:, b:b + 1], row_q[:, b * BLK * P:(b + 1) * BLK * P], AX.X)\
                    .then_inc(S["blk_max"], 1)

            def h_block(b):
                if b >= HT_BY_SCALAR:
                    dve.wait_ge(S["ht_ps"], b + 1)
                    if b >= 2:
                        dve.wait_ge(S["f2_ps"], b - 1)
                    dve.tensor_copy(h_t[b % 2], ps_t[b % 2][:, :]).then_inc(S["ht_v"], 1)
                else:
                    dve.wait_ge(S["relu_done"], BLK * (b + 1))
                dve.tensor_copy(xpair[:, b * BLK:(b + 1) * BLK, 0:F], xs[:, b * BLK:(b + 1) * BLK, :])\
                    .then_inc(S["h_hi"], 1)
                if b >= MAX_LAG:
                    block_max(b - MAX_LAG)

            for g in range(NXG // 2):
                layernorm_stats(g)
            variances(0)
            layernorm_scales(0)
            for b in range(EARLY):
                for g in range(NXG // 2 * b // EARLY, NXG // 2 * (b + 1) // EARLY):
                    layernorm_stats(NXG // 2 + g)
                h_block(b)
            variances(1)
            layernorm_scales(1)
            for b in range(EARLY, NBLK):
                h_block(b)
            done = [0]

            def then(name, op):
                done[0] += 1
                op.then_inc(S[name], 1)
                dve.wait_ge(S[name], done[0])

            dve.wait_ge(S["sig_e"], 1)
            then("coef_chain", dve.tensor_scalar(sig, sig, 1.0, None, ALU.add))
            then("coef_chain", dve.reciprocal(sig, sig))
            then("coef_chain", dve.tensor_scalar(m2s, sig[:, 2:3], -1.0 / H_SCALE, 1.0 / H_SCALE, ALU.mult, ALU.add))
            then("coef_chain", dve.tensor_scalar(nc3, sig[:, 3:4], -1.0, None, ALU.mult))
            then("coef_chain", dve.tensor_copy(c1, sig[:, 1:2]))
            then("coef_chain", dve.tensor_scalar(om1, sig[:, 1:2], -1.0, 1.0, ALU.mult, ALU.add))
            then("coef_chain", dve.tensor_scalar(om0, sig[:, 0:1], -1.0, 1.0, ALU.mult, ALU.add))
            then("coef_chain", dve.tensor_tensor(k0, om1, om0, ALU.mult))
            then("coef_chain", dve.tensor_tensor(k_a, om1, sig[:, 0:1], ALU.mult))
            for b in range(NBLK - MAX_LAG, NBLK):
                block_max(b)
            dve.wait_ge(S["blk_max"], NBLK)
            done[0] = 0
            then("gm_chain", dve.reduce_max(gmax, gblk, AX.X))
            dve.wait_ge(S["gm_ps"], 1)
            then("gm_chain", dve.tensor_scalar(ngmax, gmax_ps, -1.0, None, ALU.mult))
            then("gm_chain", dve.tensor_scalar(ngmax_q, gmax_ps, -ALPHA, None, ALU.mult))
            then("gm_chain", dve.tensor_scalar(gmax_c, gmax_ps, 1.0 - ALPHA, None, ALU.mult))
            dve.wait_ge(S["c_done"], 1)
            dve.tensor_scalar(c_all[:, :], c_all[:, :], C_MAX, None, ALU.min).then_inc(S["c_capped"], 1)
            dve.wait_ge(S["c_capped"], 1)
            dve.wait_ge(S["scratch_out"], HS_STORED)
            dve.wait_ge(S["h_lo"], NBLK)

            def step(u, k, first):
                par, g = (k // GPT) % BODY, k % GPT
                t = BODY * u + k // GPT
                slot = k % V_SLOTS
                if k < END and k % 2 == 0:
                    cs = slice(g * GROUP, g * GROUP + CHUNK)
                    if first and k < GPT:
                        dve.wait_ge(S["row_done"], g + 2)
                    if not (first and k < V_SLOTS):
                        dve.wait_ge(S["tr_done"], STEPS * u + k - V_SLOTS + 2)
                        dve.wait_ge(S["sq_done"], STEPS // 2 * u + (k - V_SLOTS) // 2 + 1)
                    dve.scalar_tensor_tensor(work[:, slot:slot + 2, :].rearrange("p a c -> p (a c)"), row_b[:, cs],
                                             c_all[:, bass.ds(t, 1)], row_q[:, cs], ALU.mult, ALU.max)\
                        .then_inc(S["t_done"], 1)
                    dve.wait_ge(S["t_done"], STEPS // 2 * u + k // 2 + 1)
                if k < END:
                    dve.wait_ge(adj_in[k % ADJ_SLOTS], 16 * (STEPS // ADJ_SLOTS * u + k // ADJ_SLOTS + 1))
                    dve.scalar_tensor_tensor(work[:, slot, :], adj_sb[:, k % ADJ_SLOTS, :], 0.0, work[:, slot, :],
                                             ALU.is_gt, ALU.mult, accum_out=vs[:, par, g:g + 1])\
                        .then_inc(S["v_done"], 1)
                if k < END and g == GPT - 1:
                    chain = S["den_chain"]
                    dve.wait_ge(S["v_done"], STEPS * u + k + 1)
                    dve.reduce_sum(vsum, vs[:, par, :], AX.X).then_inc(chain, 1)
                    dve.wait_ge(chain, 3 * t + 1)
                    dve.tensor_scalar(rbias[par], vsum, 0.0, U_SCALE / N, ALU.is_equal, ALU.mult).then_inc(chain, 1)
                    dve.wait_ge(chain, 3 * t + 2)
                    dve.scalar_tensor_tensor(wden, vsum, 1.0 / U_SCALE, rbias[par], ALU.mult, ALU.add)\
                        .then_inc(chain, 1)
                    dve.wait_ge(chain, 3 * t + 3)
                    dve.reciprocal(rnorm[par], wden).then_inc(S["r_done"], 1)
                m = k - SPLIT_LAG
                if exists(m, first) and m % GPT not in BY_SCALAR:
                    dve.wait_ge(S["hi_done"], STEPS * u + m + 1)
                    dve.tensor_tensor(pair[:, m % PAIR_SLOTS, 1, :], ps_t[m % 2][:, :], pair[:, m % PAIR_SLOTS, 0, :],
                                      ALU.subtract).then_inc(S["lo_v"], 1)
                m = k - 2 * GPT
                if exists(m, first) and g == E2_AT:
                    finish_pu(BODY * u + m // GPT, m // GPT % BODY, U_SCALE * H_SCALE, "e1_done", "pu_done")

            def finish_pu(t, par, scale, ready, done_name):
                dve.wait_ge(S[ready], t + 1)
                dve.scalar_tensor_tensor(pu[:, :], acc[par][:, 0:F], 1.0 / scale, pu[:, :], ALU.mult, ALU.add)\
                    .then_inc(S[done_name], 1)

            turns(dve, step, 2 * GPT)

            def phase2(v, par, first):
                t = 2 * v + par
                xt, h0t, ft, o = (ep[:, par, i, 0:F] for i in range(4))
                rowsum = ep[:, par, 2, F:F + 1]
                chain = S["out_chain"]

                def then(op, i):
                    op.then_inc(chain, 1)
                    dve.wait_ge(chain, 5 * t + i)

                dve.wait_ge(ep_in[par], 48 * (v + 1))
                then(dve.scalar_tensor_tensor(k_i, rowsum, c1, k_a, ALU.mult, ALU.add), 1)
                dve.wait_ge(S["e3_done"], t + 1)
                then(dve.scalar_tensor_tensor(pu[:, :], acc[1 + par][:, 0:F], 1.0 / (U_SCALE * FEAT_SCALE), pu[:, :],
                                              ALU.mult, ALU.add), 2)
                if not first:
                    dve.wait_ge(o_out[par], 16 * v)
                then(dve.scalar_tensor_tensor(ft, pu[:, :], nc3, ft, ALU.mult, ALU.add), 3)
                then(dve.scalar_tensor_tensor(o, pu[:, :], c1, xt, ALU.mult, ALU.add), 4)
                then(dve.scalar_tensor_tensor(o, ft, k_i, o, ALU.mult, ALU.add), 5)
                dve.scalar_tensor_tensor(o, h0t, k0, o, ALU.mult, ALU.add).then_inc(S["out_done"], 1)

            phase2(0, 0, True)
            phase2(0, 1, True)
            with dve.Fori(1, PAIRS) as v:
                phase2(v, 0, False)
                phase2(v, 1, False)

        @block.tensor
        def _(pe):
            pe.wait_ge(S["id_done"], 2)
            pe.wait_ge(S["a2_done"], 4)
            pe.wait_ge(S["id_done"], 3)

            def f2_block(b):
                wait_ht(pe, b)
                if b >= 2:
                    pe.wait_ge(S["f2_sb"], b - 1)
                for k in range(2):
                    last = pe.matmul(acc[b % 2][:, :], a2_wide[:, k, :], h_t[b % 2][:, k * BLK * P:(k + 1) * BLK * P],
                                     start=(k == 0), stop=(k == 1))
                last.then_inc(S["f2_ps"], 1)

            def f1_block(b):
                pe.wait_ge(S["f2_sb"], b + 1)
                for t in range(b * BLK, (b + 1) * BLK):
                    last = pe.transpose(ps_f1[:, t:t + 1], row_q[0:1, t * P:(t + 1) * P], one)
                last.then_inc(S["f1_done"], 1)

            for b in range(NBLK):
                pe.wait_ge(S["relu_done"], BLK * (b + 1))
                if b >= 2:
                    wait_ht(pe, b - 2)
                for k in range(2):
                    for i in range(BLK):
                        c0 = (k * BLK + i) * P
                        last = pe.transpose(ps_t[b % 2][:, c0:c0 + P], xs[:, b * BLK + i, k * P:(k + 1) * P], ident[:, :])
                last.then_inc(S["ht_ps"], 1)
                if b >= 1:
                    f2_block(b - 1)
                if b > F1_LAG:
                    f1_block(b - F1_LAG - 1)
            f2_block(NBLK - 1)
            for b in range(NBLK - F1_LAG - 1, NBLK):
                f1_block(b)
            pe.wait_ge(S["gm_chain"], 1)
            pe.matmul(gmax_ps, ident[:, 1:2].to_broadcast([P, P]), gmax, start=True, stop=True).then_inc(S["gm_ps"], 1)
            pe.wait_ge(S["c_done"], 1)
            pe.wait_ge(S["h_lo"], NBLK)

            def products(bank, high, low, feats, start, stop):
                whole = lambda stop: pe.matmul(bank[:, :], high, feats, start=start, stop=stop)
                half = lambda: pe.matmul(bank[:, 0:F], low, feats[:, 0:F], start=False, stop=False)
                if stop:
                    half()
                    return whole(True)
                whole(False)
                return half()

            def step(u, k, first):
                if k < END:
                    if k % 2 == 0:
                        pe.wait_ge(S["norm_done"], STEPS // 2 * u + k // 2 + 1)
                    if not (first and k < 2):
                        wait_lo(pe, u, k - 2)
                    for q in range(QPG):
                        last = pe.matmul(ps_t[k % 2][:, q * P:(q + 1) * P], work[:, k % V_SLOTS, q * P:(q + 1) * P],
                                         ident[:, :], is_transpose=True, start=(q % 4 == 0), stop=(q % 4 == 3))
                    last.then_inc(S["tr_done"], 1)
                m = k - 1
                if exists(m, first) and m % GPT in BY_SCALAR:
                    pe.wait_ge(S["hi_done"], STEPS * u + m + 1)
                    for q in range(2):
                        qs = slice(q * 4 * P, (q + 1) * 4 * P)
                        last = pe.matmul(ps_t[m % 2][:, qs], neg_ident[:, :], pair[:, m % PAIR_SLOTS, 0, qs],
                                         start=False, stop=True, skip_group_check=True)
                    last.then_inc(S["res_done"], 1)
                m = k - MM_LAG
                if exists(m, first):
                    par, g = m // GPT % BODY, m % GPT
                    wait_lo(pe, u, m)
                    if g == 0 and not (first and m < BODY * GPT):
                        pe.wait_ge(S["pu_done"], BODY * u + m // GPT - BODY + 1)
                    for q in range(QPG):
                        j = g * QPG + q
                        last = products(acc[par], pair[:, m % PAIR_SLOTS, 0, q * P:(q + 1) * P],
                                        pair[:, m % PAIR_SLOTS, 1, q * P:(q + 1) * P], xpair[:, j, :],
                                        j == 0, j == TILES - 1)
                    last.then_inc(S["mm_done"], 1)

            turns(pe, step, MM_LAG)

            def phase2(v, par, first):
                t = 2 * v + par
                for q in range(QPT):
                    slot = par * QPT + q
                    if first and par == 0:
                        pe.wait_ge(fx_in[2 * q], 16)
                        pe.wait_ge(fx_in[2 * q + 1], 16)
                    if q == 0:
                        if first:
                            pe.wait_ge(S["pu_done"], TILES - 1)
                        else:
                            pe.wait_ge(S["out_done"], t - 1)
                    pe.wait_ge(ut_in[slot], 16 * (v + 1))
                    for i in range(2 * QPG):
                        j = q * 2 * QPG + i
                        c0 = (i // QPG) * 2 * GROUP + (i % QPG) * P
                        last = products(acc[1 + par], ut_sb[:, slot, c0:c0 + P], ut_sb[:, slot, c0 + GROUP:c0 + GROUP + P],
                                        fx[:, j, :], j == 0, j == TILES - 1)
                    last.then_inc(S["mm2_done"], 1)

            phase2(0, 0, True)
            phase2(0, 1, True)
            with pe.Fori(1, PAIRS) as v:
                phase2(v, 0, False)
                phase2(v, 1, False)


def kernel(x, adj, L0_gnn_h0, L0_gnn_a, L0_gnn_temp):
    import numpy as _np
    import concourse.bacc as _bacc
    from concourse import mybir as _mybir
    from concourse.bass_utils import run_bass_kernel_spmd as _run

    nc = _bacc.Bacc("TRN2", target_bir_lowering=False, num_devices=1, dynamic_dma_scratch_size=1024)
    given = {"x": x, "adj": adj, "h0": L0_gnn_h0, "a": L0_gnn_a, "temp": L0_gnn_temp}
    arrays, args = {}, []
    for name, value in given.items():
        v = _np.ascontiguousarray(value)
        arrays[f"in_{name}"] = v
        args.append(nc.dram_tensor(f"in_{name}", v.shape, _mybir.dt.from_np(v.dtype), kind="ExternalInput").ap())
    out = nc.dram_tensor("out_0", x.shape, _mybir.dt.float32, kind="ExternalOutput").ap()
    graph_attention_layer(nc, *args, out)
    r = _run(nc, [arrays], core_ids=[0])
    return r.results[0]["out_0"]
```
